# Optimizing a Trainium2 kernel written in Bass

```python
import numpy as np
import jax
import jax.numpy as jnp

def _softmax(x, axis=-1):
    return jax.nn.softmax(x, axis=axis)

def _gelu(x):
    return jax.nn.gelu(x, approximate=True)

def _silu(x):
    return jax.nn.silu(x)

def _sigmoid(x):
    return jax.nn.sigmoid(x)

def _layernorm(x, axis=-1, eps=1e-05):
    m = jnp.mean(x, axis=axis, keepdims=True)
    v = jnp.var(x, axis=axis, keepdims=True)
    return (x - m) / jnp.sqrt(v + eps)

def _scatter_add(tgt, idx, src, axis=0):
    return tgt.at[idx].add(src)

def _segment_sum(src, seg, n):
    return jax.ops.segment_sum(src, seg, n)
kernel_name = 'mk_seq_preln_d2_jaxref_r8_88265c'

def setup_inputs(seed: int=0):
    np.random.seed(seed)
    _w = jnp.asarray

    def _L0_attn_setup():
        import jax, jax.numpy as jnp
        import numpy as np
        BATCH, SEQ, HIDDEN = (2, 512, 512)
        HEADS, HEAD_DIM, BLOCK = (32, 128, 32)
        LAYER_IDX, N_LAYERS = (1, 32)
        EPS = 1e-05

        def _decays():
            base = 1.0 / 2.0 ** (8.0 / HEADS)
            exponent = jnp.arange(HEADS, dtype=jnp.float32) + 1.0
            factor = 1.0 - LAYER_IDX / (N_LAYERS - 1 + 1e-05) + 1e-05
            slope = (base ** exponent * factor)[:, None, None]
            r = jnp.arange(BLOCK, dtype=jnp.float32) + 1.0
            q_decay = jnp.exp(-slope * r[:, None])
            k_decay = jnp.exp(-slope * (BLOCK - r)[:, None])
            diff = r[:, None] - r[None, :]
            diag = slope[None] * diff[None, None]
            diag = jnp.where(diag >= 0, -diag, -jnp.inf)
            diag_decay = jnp.exp(diag)
            block_decay = jnp.exp(-slope * BLOCK)
            return (q_decay, k_decay, diag_decay, block_decay)
        key = jax.random.key(seed)
        ks = jax.random.split(key, 5)
        s = 0.02
        return {'hidden_states': jax.random.normal(ks[0], (BATCH, SEQ, HIDDEN), jnp.float32), 'qkv_w': jax.random.normal(ks[1], (3 * HEADS * HEAD_DIM, HIDDEN), jnp.float32) * s, 'out_w': jax.random.normal(ks[2], (HIDDEN, HEADS * HEAD_DIM), jnp.float32) * s, 'gate_w': jax.random.normal(ks[3], (HEADS * HEAD_DIM, HIDDEN), jnp.float32) * s, 'norm_w': jnp.ones((HEADS * HEAD_DIM,), jnp.float32)}
    _L0_attn_in = _L0_attn_setup()

    def _L0_ffn_setup():
        import jax, jax.numpy as jnp
        import numpy as np
        DIM = 512
        HID = 1376
        R = 16
        SCALING = 32.0 / 16.0

        def _lora_linear(x, w, a, b):
            base = jnp.einsum('bsd,od->bso', x, w)
            low = jnp.einsum('bsr,or->bso', jnp.einsum('bsd,rd->bsr', x, a), b)
            return base + low * SCALING
        key = jax.random.key(seed)
        ks = jax.random.split(key, 10)
        s_in = 1.0 / np.sqrt(DIM)
        s_hid = 1.0 / np.sqrt(HID)
        return {'x': jax.random.normal(ks[0], (4, 256, DIM), jnp.float32), 'w1': jax.random.normal(ks[1], (HID, DIM), jnp.float32) * s_in, 'w3': jax.random.normal(ks[2], (HID, DIM), jnp.float32) * s_in, 'w2': jax.random.normal(ks[3], (DIM, HID), jnp.float32) * s_hid, 'lora_A1': jax.random.normal(ks[4], (R, DIM), jnp.float32) * s_in, 'lora_B1': jax.random.normal(ks[5], (HID, R), jnp.float32) * 0.02, 'lora_A3': jax.random.normal(ks[6], (R, DIM), jnp.float32) * s_in, 'lora_B3': jax.random.normal(ks[7], (HID, R), jnp.float32) * 0.02, 'lora_A2': jax.random.normal(ks[8], (R, HID), jnp.float32) * s_hid, 'lora_B2': jax.random.normal(ks[9], (DIM, R), jnp.float32) * 0.02}
    _L0_ffn_in = _L0_ffn_setup()

    def _L1_attn_setup():
        import jax, jax.numpy as jnp
        import numpy as np
        import math
        D_MODEL = 512
        N_HEADS = 32
        HEAD_DIM = D_MODEL // N_HEADS
        CLIP_QKV = 8.0
        ALIBI_BIAS_MAX = 8
        LN_EPS = 1e-05

        def _alibi_slopes(total_num_heads: int, alibi_bias_max: int) -> jnp.ndarray:
            next_p2 = 2 ** math.ceil(math.log2(total_num_heads))
            m = jnp.arange(1, next_p2 + 1, dtype=jnp.float32) * (alibi_bias_max / next_p2)
            slopes = 1.0 / jnp.power(2.0, m)
            if next_p2 != total_num_heads:
                slopes = jnp.concatenate([slopes[1::2], slopes[::2]])[:total_num_heads]
            return slopes

        def _layer_norm(x, w, b):
            mu = jnp.mean(x, axis=-1, keepdims=True)
            var = jnp.var(x, axis=-1, keepdims=True)
            return (x - mu) * jax.lax.rsqrt(var + LN_EPS) * w + b
        key = jax.random.key(seed)
        k0, k1, k2 = jax.random.split(key, 3)
        B, S = (2, 256)
        return {'hidden_states': jax.random.normal(k0, (B, S, D_MODEL), dtype=jnp.float32), 'w_qkv': jax.random.normal(k1, (3 * D_MODEL, D_MODEL), dtype=jnp.float32) * 0.02, 'q_ln_w': jnp.ones((D_MODEL,), jnp.float32), 'q_ln_b': jnp.zeros((D_MODEL,), jnp.float32), 'k_ln_w': jnp.ones((D_MODEL,), jnp.float32), 'k_ln_b': jnp.zeros((D_MODEL,), jnp.float32), 'w_out': jax.random.normal(k2, (D_MODEL, D_MODEL), dtype=jnp.float32) * 0.02}
    _L1_attn_in = _L1_attn_setup()

    def _L1_ffn_setup():
        import jax, jax.numpy as jnp
        import numpy as np
        B, S, D, F = (4, 256, 512, 2048)
        key = jax.random.key(seed)
        k = jax.random.split(key, 5)
        scale_in = 1.0 / np.sqrt(D)
        scale_out = 1.0 / np.sqrt(F)
        return {'input': jax.random.normal(k[0], (B, S, D), dtype=jnp.float32), 'inter_w': jax.random.normal(k[1], (D, F), dtype=jnp.float32) * scale_in, 'inter_b': jax.random.normal(k[2], (F,), dtype=jnp.float32) * 0.02, 'output_w': jax.random.normal(k[3], (F, D), dtype=jnp.float32) * scale_out, 'output_b': jax.random.normal(k[4], (D,), dtype=jnp.float32) * 0.02}
    _L1_ffn_in = _L1_ffn_setup()
    _d = {'L0_attn_hidden_states': _L0_attn_in['hidden_states'], 'L0_attn_qkv_w': _L0_attn_in['qkv_w'], 'L0_attn_out_w': _L0_attn_in['out_w'], 'L0_attn_gate_w': _L0_attn_in['gate_w'], 'L0_attn_norm_w': _L0_attn_in['norm_w'], 'L0_ffn_w1': _L0_ffn_in['w1'], 'L0_ffn_w3': _L0_ffn_in['w3'], 'L0_ffn_w2': _L0_ffn_in['w2'], 'L0_ffn_lora_A1': _L0_ffn_in['lora_A1'], 'L0_ffn_lora_B1': _L0_ffn_in['lora_B1'], 'L0_ffn_lora_A3': _L0_ffn_in['lora_A3'], 'L0_ffn_lora_B3': _L0_ffn_in['lora_B3'], 'L0_ffn_lora_A2': _L0_ffn_in['lora_A2'], 'L0_ffn_lora_B2': _L0_ffn_in['lora_B2'], 'L1_attn_w_qkv': _L1_attn_in['w_qkv'], 'L1_attn_q_ln_w': _L1_attn_in['q_ln_w'], 'L1_attn_q_ln_b': _L1_attn_in['q_ln_b'], 'L1_attn_k_ln_w': _L1_attn_in['k_ln_w'], 'L1_attn_k_ln_b': _L1_attn_in['k_ln_b'], 'L1_attn_w_out': _L1_attn_in['w_out'], 'L1_ffn_inter_w': _L1_ffn_in['inter_w'], 'L1_ffn_inter_b': _L1_ffn_in['inter_b'], 'L1_ffn_output_w': _L1_ffn_in['output_w'], 'L1_ffn_output_b': _L1_ffn_in['output_b']}
    _x0 = _d['L0_attn_hidden_states']
    _d['L0_attn_hidden_states'] = jax.random.normal(jax.random.fold_in(jax.random.key(seed), 1), (1, 1024, 512), dtype=_x0.dtype)
    del _x0
    return _d

def reference(L0_attn_hidden_states, L0_attn_qkv_w, L0_attn_out_w, L0_attn_gate_w, L0_attn_norm_w, L0_ffn_w1, L0_ffn_w3, L0_ffn_w2, L0_ffn_lora_A1, L0_ffn_lora_B1, L0_ffn_lora_A3, L0_ffn_lora_B3, L0_ffn_lora_A2, L0_ffn_lora_B2, L1_attn_w_qkv, L1_attn_q_ln_w, L1_attn_q_ln_b, L1_attn_k_ln_w, L1_attn_k_ln_b, L1_attn_w_out, L1_ffn_inter_w, L1_ffn_inter_b, L1_ffn_output_w, L1_ffn_output_b):

    def _L0_attn_ref(hidden_states, qkv_w, out_w, gate_w, norm_w):
        import jax, jax.numpy as jnp
        import numpy as np
        BATCH, SEQ, HIDDEN = (2, 512, 512)
        HEADS, HEAD_DIM, BLOCK = (32, 128, 32)
        LAYER_IDX, N_LAYERS = (1, 32)
        EPS = 1e-05

        def _decays():
            base = 1.0 / 2.0 ** (8.0 / HEADS)
            exponent = jnp.arange(HEADS, dtype=jnp.float32) + 1.0
            factor = 1.0 - LAYER_IDX / (N_LAYERS - 1 + 1e-05) + 1e-05
            slope = (base ** exponent * factor)[:, None, None]
            r = jnp.arange(BLOCK, dtype=jnp.float32) + 1.0
            q_decay = jnp.exp(-slope * r[:, None])
            k_decay = jnp.exp(-slope * (BLOCK - r)[:, None])
            diff = r[:, None] - r[None, :]
            diag = slope[None] * diff[None, None]
            diag = jnp.where(diag >= 0, -diag, -jnp.inf)
            diag_decay = jnp.exp(diag)
            block_decay = jnp.exp(-slope * BLOCK)
            return (q_decay, k_decay, diag_decay, block_decay)
        b, s, _ = hidden_states.shape
        h, d, bs = (HEADS, HEAD_DIM, BLOCK)
        nb = s // bs
        q_decay, k_decay, diag_decay, block_decay = _decays()
        qkv = jax.nn.silu(hidden_states @ qkv_w.T)
        qkv = qkv.reshape(b, s, h, 3, d)
        q = jnp.moveaxis(qkv[:, :, :, 0], 2, 1)
        k = jnp.moveaxis(qkv[:, :, :, 1], 2, 1)
        v = jnp.moveaxis(qkv[:, :, :, 2], 2, 1)

        def to_blocks(x):
            return jnp.moveaxis(x.reshape(b, h, nb, bs, d), 2, 0)
        qb, kb, vb = (to_blocks(q), to_blocks(k), to_blocks(v))

        def step(kv, blk):
            cq, ck, cv = blk
            scores = jnp.einsum('bhnd,bhmd->bhnm', cq, ck) * diag_decay
            intra = jnp.einsum('bhnm,bhmd->bhnd', scores, cv)
            inter = jnp.einsum('bhnd,bhde->bhne', cq * q_decay, kv)
            kv_next = kv * block_decay + jnp.einsum('bhnd,bhne->bhde', ck * k_decay, cv)
            return (kv_next, intra + inter)
        kv0 = jnp.zeros((b, h, d, d), hidden_states.dtype)
        _, out_blocks = jax.lax.scan(step, kv0, (qb, kb, vb))
        attn = jnp.moveaxis(out_blocks, 0, 2)
        attn = attn.reshape(b, h, s, d).transpose(0, 2, 1, 3).reshape(b, s, h * d)
        xf = attn.astype(jnp.float32)
        xf = xf * jax.lax.rsqrt(jnp.mean(xf * xf, axis=-1, keepdims=True) + EPS)
        normed = norm_w * xf.astype(attn.dtype)
        gate = jax.nn.sigmoid(hidden_states @ gate_w.T)
        return gate * normed @ out_w.T

    def _L0_ffn_ref(x, w1, w3, w2, lora_A1, lora_B1, lora_A3, lora_B3, lora_A2, lora_B2):
        import jax, jax.numpy as jnp
        import numpy as np
        DIM = 512
        HID = 1376
        R = 16
        SCALING = 32.0 / 16.0

        def _lora_linear(x, w, a, b):
            base = jnp.einsum('bsd,od->bso', x, w)
            low = jnp.einsum('bsr,or->bso', jnp.einsum('bsd,rd->bsr', x, a), b)
            return base + low * SCALING
        h1 = _lora_linear(x, w1, lora_A1, lora_B1)
        h3 = _lora_linear(x, w3, lora_A3, lora_B3)
        g = jax.nn.silu(h1) * h3
        return _lora_linear(g, w2, lora_A2, lora_B2)

    def _L1_attn_ref(hidden_states, w_qkv, q_ln_w, q_ln_b, k_ln_w, k_ln_b, w_out):
        import jax, jax.numpy as jnp
        import numpy as np
        import math
        D_MODEL = 512
        N_HEADS = 32
        HEAD_DIM = D_MODEL // N_HEADS
        CLIP_QKV = 8.0
        ALIBI_BIAS_MAX = 8
        LN_EPS = 1e-05

        def _alibi_slopes(total_num_heads: int, alibi_bias_max: int) -> jnp.ndarray:
            next_p2 = 2 ** math.ceil(math.log2(total_num_heads))
            m = jnp.arange(1, next_p2 + 1, dtype=jnp.float32) * (alibi_bias_max / next_p2)
            slopes = 1.0 / jnp.power(2.0, m)
            if next_p2 != total_num_heads:
                slopes = jnp.concatenate([slopes[1::2], slopes[::2]])[:total_num_heads]
            return slopes

        def _layer_norm(x, w, b):
            mu = jnp.mean(x, axis=-1, keepdims=True)
            var = jnp.var(x, axis=-1, keepdims=True)
            return (x - mu) * jax.lax.rsqrt(var + LN_EPS) * w + b
        B, S, D = hidden_states.shape
        qkv = jnp.einsum('bsd,ed->bse', hidden_states, w_qkv)
        qkv = jnp.clip(qkv, -CLIP_QKV, CLIP_QKV)
        q, k, v = jnp.split(qkv, 3, axis=-1)
        q = _layer_norm(q, q_ln_w, q_ln_b)
        k = _layer_norm(k, k_ln_w, k_ln_b)
        q = q.reshape(B, S, N_HEADS, HEAD_DIM)
        k = k.reshape(B, S, N_HEADS, HEAD_DIM)
        v = v.reshape(B, S, N_HEADS, HEAD_DIM)
        scale = HEAD_DIM ** (-0.5)
        scores = jnp.einsum('bqhd,bkhd->bhqk', q, k) * scale
        pos = jnp.arange(S)
        rel = pos[None, :] - pos[:, None]
        slopes = _alibi_slopes(N_HEADS, ALIBI_BIAS_MAX)
        bias = slopes[:, None, None] * rel.astype(jnp.float32)
        causal = rel <= 0
        scores = jnp.where(causal[None, None], scores + bias[None], -jnp.inf)
        probs = jax.nn.softmax(scores, axis=-1)
        attn = jnp.einsum('bhqk,bkhd->bqhd', probs, v).reshape(B, S, D)
        return jnp.einsum('bsd,ed->bse', attn, w_out)

    def _L1_ffn_ref(input, inter_w, inter_b, output_w, output_b):
        import jax, jax.numpy as jnp
        import numpy as np
        B, S, D, F = (4, 256, 512, 2048)
        h = jax.nn.gelu(jnp.einsum('bsd,df->bsf', input, inter_w) + inter_b, approximate=True)
        out = jnp.einsum('bsf,fd->bsd', h, output_w) + output_b
        return out
    x = L0_attn_hidden_states
    x = x + _L0_attn_ref(_layernorm(x, axis=-1), L0_attn_qkv_w, L0_attn_out_w, L0_attn_gate_w, L0_attn_norm_w)
    x = x + _L0_ffn_ref(_layernorm(x, axis=-1), L0_ffn_w1, L0_ffn_w3, L0_ffn_w2, L0_ffn_lora_A1, L0_ffn_lora_B1, L0_ffn_lora_A3, L0_ffn_lora_B3, L0_ffn_lora_A2, L0_ffn_lora_B2)
    x = x + _L1_attn_ref(_layernorm(x, axis=-1), L1_attn_w_qkv, L1_attn_q_ln_w, L1_attn_q_ln_b, L1_attn_k_ln_w, L1_attn_k_ln_b, L1_attn_w_out)
    x = x + _L1_ffn_ref(_layernorm(x, axis=-1), L1_ffn_inter_w, L1_ffn_inter_b, L1_ffn_output_w, L1_ffn_output_b)
    return x

_drawn_inputs = setup_inputs


def setup_inputs(seed=0):
    import zlib

    import numpy as np

    out = dict(_drawn_inputs(seed))
    spreads = {'L0_attn_norm_w': (1.0, 0.2),
     'L1_attn_q_ln_w': (1.0, 0.6),
     'L1_attn_q_ln_b': (0.0, 0.8),
     'L1_attn_k_ln_w': (1.0, 0.6),
     'L1_attn_k_ln_b': (0.0, 0.8)}
    factors = {'L1_ffn_inter_b': 6.651, 'L1_ffn_output_b': 4.647}
    for name, (base, spread) in spreads.items():
        noise = np.random.default_rng([zlib.crc32(name.encode()), seed]).standard_normal(out[name].shape)
        drawn = base * np.exp(spread * noise) if base else spread * noise
        out[name] = jnp.asarray(drawn.astype(out[name].dtype))
    for name, factor in factors.items():
        out[name] = (out[name] * factor).astype(out[name].dtype)
    return out
```

```python
import concourse.bass as bass
from concourse import mybir
from contextlib import ExitStack

F32 = mybir.dt.float32
F32R = mybir.dt.float32r
BF16 = mybir.dt.bfloat16
ALU = mybir.AluOpType
ACT = mybir.ActivationFunctionType
AX = mybir.AxisListType

P = 128
T = 1024
NT = T // P
D = 512
KT = D // P
BANK = 512
EPS = 1e-5

H0, DH0 = 32, 128
G4 = 4
NG = H0 // G4
NC = T // P
CST = 2 * P + 2
W4 = 4 * 512

F0 = 1376
NF0 = -(-F0 // P)
LR = 96
LORA_SCALE = 2.0

H1, DH1 = 32, 16
CLIP = 8.0

F1 = 2048
NF1 = F1 // P


def split_hi(engine, hi, src):
    return engine.tensor_scalar(hi, src, 1.0, 0.0, ALU.mult, ALU.add)


def take_wait(nc, top, step):
    if not isinstance(step, int):
        nc.gpsimd.tensor_tensor(top["tick"][:, :], top["neg_half"][:, 0:1], top["neg_half"][:, 1:2], ALU.mult)


class Sems:

    def __init__(self, nc, ctx, stage):
        self._nc, self._stage, self._known = nc, stage, {}
        ctx.callback(self._clear)

    def __call__(self, name):
        if name not in self._known:
            self._known[name] = self._nc.alloc_semaphore(name=f"{self._stage}_{name}")
        return self._known[name]

    def _clear(self):
        self._nc.clear_and_free_semaphores(list(self._known.values()))
        self._nc.all_engine_barrier()



def ln_vector(nc, dve, s, b, x_ready=None):
    ahead = 3

    def stats(t):
        if x_ready is not None:
            dve.wait_ge(*x_ready(t))
        nc.vector.bn_stats(b["stats"][:, t, :], b["x"][:, t, :]).then_inc(s("ln_stats"), 1)
        dve.wait_ge(s("ln_stats"), t + 1)
        nc.vector.bn_aggr(b["meanvar"][:, t, :], b["stats"][:, t, :]).then_inc(s("ln_meanvar"), 1)

    for t in range(ahead):
        stats(t)
    for t in range(NT):
        if t + ahead < NT:
            stats(t + ahead)
        dve.wait_ge(s("ln_hi"), t + 1)
        nc.vector.tensor_tensor(b["xh_l"][:, :, t * P:(t + 1) * P],
                                b["ps"][:, t, :].rearrange("p (k q) -> p k q", k=KT),
                                b["xh_h"][:, :, t * P:(t + 1) * P], ALU.subtract).then_inc(s("ln_lo"), 1)


def ln_gpsimd(nc, pool, s, b, t):
    one = slice(t, t + 1)
    pool.wait_ge(s("ln_meanvar"), t + 1)
    nc.gpsimd.tensor_scalar(b["var_eps"][:, one], b["meanvar"][:, t, 1:2], 1.0, EPS, ALU.mult, ALU.add
                            ).then_inc(s("ln_var_eps"), 1)
    pool.wait_ge(s("ln_var_eps"), t + 1)
    nc.gpsimd.tensor_tensor(b["rstd"][:, one], b["var_eps"][:, one], b["neg_half"][:, one], ALU.pow
                            ).then_inc(s("ln_rstd"), 1)
    pool.wait_ge(s("ln_rstd"), t + 1)
    nc.gpsimd.tensor_scalar(b["shift"][:, one], b["meanvar"][:, t, 0:1], b["rstd"][:, one], -1.0, ALU.mult, ALU.mult
                            ).then_inc(s("ln_shift"), 1)


def ln_scalar(nc, act, s, b):
    for t in range(NT + 1):
        if t < NT:
            act.wait_ge(s("ln_shift"), t + 1)
            if t >= 2:
                act.wait_ge(s("ln_transposed"), t - 1)
            nc.scalar.activation(b["xn"][:, t % 2, :], b["x"][:, t, :], ACT.Identity, bias=b["shift"][:, t:t + 1],
                                 scale=b["rstd"][:, t:t + 1]).then_inc(s("ln_normed"), 1)
        if t >= 1:
            u = t - 1
            act.wait_ge(s("ln_transposed"), u + 1)
            nc.scalar.copy(b["xh_h"][:, :, u * P:(u + 1) * P],
                           b["ps"][:, u, :].rearrange("p (k q) -> p k q", k=KT)).then_inc(s("ln_hi"), 1)


def ln_tensor(nc, pe, s, b, tiles):
    for t in tiles:
        pe.wait_ge(s("ln_normed"), t + 1)
        for k in range(KT):
            last = nc.tensor.transpose(b["ps"][:, t, k * P:(k + 1) * P], b["xn"][:, t % 2, k * P:(k + 1) * P],
                                       b["ident"][:, :])
        last.then_inc(s("ln_transposed"), 1)


def mm3(nc, out, w_hi, w_lo, x_hi, x_lo, start, stop):
    nc.tensor.matmul(out, w_hi, x_hi, start=start, stop=False)
    nc.tensor.matmul(out, w_hi, x_lo, start=False, stop=False)
    return nc.tensor.matmul(out, w_lo, x_hi, start=False, stop=stop)


def stage_attention0(nc, top, x_dram, wqkgv, wout, cst_dram, normw_dram):
    ctx = ExitStack()
    with ctx:
        def sb(name, shape, dt=F32):
            return ctx.enter_context(nc.sbuf_tensor(f"a0_{name}", shape, dt))
        s = Sems(nc, ctx, "a0")
        ps = ctx.enter_context(nc.psum_tensor("a0_ps", [P, 8, BANK], F32))
        flat = ps[:, :, :].rearrange("p b c -> p (b c)")
        UNIT = [flat[:, 0:1024], flat[:, 1024:2048]]
        TU = flat[:, 2048:3072]
        SC = flat[:, 3072:4096]

        xh_h, xh_l = sb("xh_h", [P, KT, T], F32R), sb("xh_l", [P, KT, T], F32R)
        raw = sb("raw", [P, W4 + 512])
        w_h, w_l = sb("w_h", [P, G4, W4], F32R), sb("w_l", [P, G4, W4], F32R)
        o_h, o_l = sb("o_h", [P, 2, 512], F32R), sb("o_l", [P, 2, 512], F32R)
        cst = sb("cst", [P, 2, CST])
        nw = sb("nw", [P, H0])
        nw_half = sb("nw_half", [P, H0])
        v_nat = sb("v_nat", [P, NT, G4 * DH0])
        qT, kT, qdT = sb("qT", [P, T]), sb("kT", [P, T]), sb("qdT", [P, T])
        k_nat = sb("k_nat", [P, NC, P])
        sd = sb("sd", [P, NC, P])
        state = sb("state", [P, NC - 1, P])
        th = sb("th", [P, T])
        gt = sb("gt", [P, T])
        g_h, g_l = sb("g_h", [P, 2, T], F32R), sb("g_l", [P, 2, T], F32R)
        sq, sq_sum = sb("sq", [P, T]), sb("sq_sum", [P, T])
        ms = sb("ms", [P, NT])
        rms = sb("rms", [P, NT])
        ones = sb("ones", [P, 1])
        x = acc = top["x"]
        x_again = v_nat
        early = [v_nat[:, 4 * i:4 * i + 4, :].rearrange("p a b -> p (a b)") for i in range(2)]
        b = dict(top, ps=ps, xh_h=xh_h, xh_l=xh_l, xn=gt[:, :].rearrange("p (a b) -> p a b", a=2))
        ident = top["ident"]
        heads_of = lambda ap: ap.rearrange("p (c q) -> p c q", c=NC)
        block = ctx.enter_context(nc.Block())

        PROJ = [0, 7, 10, 13]
        Q_UNIT, K_UNIT, G_UNIT = [0, 1, 0, 1], [1, 0, 1, 0], [0, 1, 0, 1]

        @block.sync
        def _(sp):
            for t in range(NT):
                sp.dma_start(x[:, t, :], x_dram[t * P:(t + 1) * P, :]).then_inc(s(f"x_in{t}"), 16)
            sp.dma_start(ident[:, :], top["ident_dram"]).then_inc(s("ident_in"), 16)
            sp.dma_start(nw[:, :], normw_dram).then_inc(s("nw_in"), 16)

            def load_weights(g, j, split=None):
                sp.wait_ge(s("w_ready"), g * G4 + j if split is None else split)
                sp.dma_start(raw[:, 0:W4], wqkgv[g, j]).then_inc(s("raw_in"), 16)

            def load_out(g, j):
                sp.wait_ge(s("o_ready"), g * G4 + j)
                sp.dma_start(raw[:, W4:W4 + 512], wout[g, j]).then_inc(s("rawo_in"), 16)

            load_weights(0, 0)
            for j in (1, 2):
                sp.dma_start(early[j - 1], wqkgv[0, j]).then_inc(s(f"early_in{j}"), 16)
            load_weights(0, 3, 1)
            for j in range(2):
                sp.dma_start(cst[:, j, :], cst_dram[0, j]).then_inc(s(f"cst_in{j}"), 16)

            def step(g, j, more):
                if more:
                    load_weights(g + 1, j)
                load_out(g, j)
                if more or j < 2:
                    sp.wait_ge(s("state_done"), g * G4 + j + 1)
                    sp.dma_start(cst[:, j % 2, :], cst_dram[g + (j + 2) // G4, (j + 2) % G4]
                                 ).then_inc(s(f"cst_in{j % 2}"), 16)

            for j in range(G4):
                step(0, j, True)
            with sp.Fori(1, NG - 1) as g:
                for j in range(G4):
                    step(g, j, True)
            for j in range(G4):
                step(NG - 1, j, False)
            sp.wait_ge(s("attn_done"), H0)
            sp.dma_start(x_again[:, :, :], x_dram.rearrange("(t p) d -> p t d", p=P)).then_inc(s("x_again_in"), 16)

        @block.gpsimd
        def _(pool):
            nc.gpsimd.memset(top["neg_half"][:, :], -0.5).then_inc(s("pool_const"), 1)
            pool.wait_ge(s("pool_const"), 1)

            def split_weights(g, j):
                m = g * G4 + j
                nth = 1 if isinstance(m, int) and m == 0 else m - 1
                pool.wait_ge(s("raw_in"), 16 * nth)
                take_wait(nc, top, g)
                split_hi(nc.gpsimd, w_h[:, j, :], raw[:, 0:W4]).then_inc(s("w_hi"), 1)
                pool.wait_ge(s("w_hi"), nth)
                nc.gpsimd.tensor_tensor(w_l[:, j, :], raw[:, 0:W4], w_h[:, j, :], ALU.subtract
                                        ).then_inc(s("w_ready"), 1)

            def split_out(g, j):
                m = g * G4 + j
                pool.wait_ge(s("rawo_in"), 16 * m + 16)
                take_wait(nc, top, g)
                split_hi(nc.gpsimd, o_h[:, j % 2, :], raw[:, W4:W4 + 512]).then_inc(s("o_hi"), 1)
                pool.wait_ge(s("o_hi"), m + 1)
                nc.gpsimd.tensor_tensor(o_l[:, j % 2, :], raw[:, W4:W4 + 512], o_h[:, j % 2, :], ALU.subtract
                                        ).then_inc(s("o_ready"), 1)

            for t in range(NT):
                ln_gpsimd(nc, pool, s, b, t)
                if t == 3:
                    split_weights(0, 0)
            split_weights(0, 3)

            def step(g, j, more):
                pool.wait_ge(s("proj_done"), 16 * g + [7, 10, 13, 16][j])
                if more:
                    split_weights(g + 1, j)
                pool.wait_ge(s("out_done"), 8 * g + (4 if j >= 2 else 0))
                split_out(g, j)

            for j in range(G4):
                step(0, j, True)
            with pool.Fori(1, NG - 1) as g:
                for j in range(G4):
                    step(g, j, True)
            for j in range(G4):
                step(NG - 1, j, False)
            pool.wait_ge(s("ms_ready"), 1)
            nc.gpsimd.tensor_tensor(rms[:, :], ms[:, :], top["neg_half"][:, 0:NT], ALU.pow
                                    ).then_inc(s("rms_ready"), 1)

        @block.scalar
        def _(act):
            ln_scalar(nc, act, s, b)

            def square(n):
                act.wait_ge(s("attn_done"), n)
                act.wait_ge(s("sq_added"), n - 1)
                nc.scalar.activation(sq[:, :], SC, ACT.Square).then_inc(s("squared"), 1)

            def step(g, j, first):
                n = g * G4 + j
                done = 16 * g + PROJ[j]
                act.wait_ge(s("proj_done"), done + 1)
                if not first:
                    act.wait_ge(s("scores_done"), n)
                    act.wait_ge(s("q_decayed"), n)
                nc.scalar.activation(qT[:, :], UNIT[Q_UNIT[j]], ACT.Silu).then_inc(s("q_ready"), 1)
                act.wait_ge(s("proj_done"), done + 2)
                nc.scalar.activation(kT[:, :], UNIT[K_UNIT[j]], ACT.Silu).then_inc(s("k_ready"), 1)
                if not first:
                    square(n)
                if j == 0:
                    for i in range(4):
                        act.wait_ge(s("proj_done"), done + 3 + i)
                        nc.scalar.activation(v_nat[:, 2 * i:2 * i + 2, :].rearrange("p a b -> p (a b)"),
                                             UNIT[i % 2], ACT.Silu).then_inc(s("v_ready"), 1)
                act.wait_ge(s("proj_done"), done + (7 if j == 0 else 3))
                if not first:
                    act.wait_ge(s("gated"), n)
                nc.scalar.activation(th[:, :], UNIT[G_UNIT[j]], ACT.Tanh, scale=0.5).then_inc(s("gate_ready"), 1)

            for j in range(G4):
                step(0, j, j == 0)
            with act.Fori(1, NG) as g:
                for j in range(G4):
                    step(g, j, False)
            square(H0)

        @block.vector
        def _(dve):
            nc.vector.memset(ones[:, :], 1.0).then_inc(s("dve_const"), 1)
            nc.vector.memset(sq_sum[:, :], 0.0).then_inc(s("dve_const"), 1)
            ln_vector(nc, dve, s, b, lambda t: (s(f"x_in{t}"), 16))
            dve.wait_ge(s("w_ready"), 1)
            for j in (1, 2):
                dve.wait_ge(s(f"early_in{j}"), 16)
                nc.vector.tensor_copy(w_h[:, j, :], early[j - 1]).then_inc(s("early_hi"), 1)
                dve.wait_ge(s("early_hi"), j)
                nc.vector.tensor_tensor(w_l[:, j, :], early[j - 1], w_h[:, j, :], ALU.subtract
                                        ).then_inc(s("w_ready"), 1)
            dve.wait_ge(s("nw_in"), 16)
            nc.vector.tensor_scalar(nw_half[:, :], nw[:, :], 0.5, None, ALU.mult).then_inc(s("dve_const"), 1)
            dve.wait_ge(s("ln_normed"), NT)
            nc.vector.memset(acc[:, :, :], 0.0).then_inc(s("dve_const"), 1)
            dve.wait_ge(s("dve_const"), 4)

            def states(n, jp):
                dve.wait_ge(s("updates_done"), n)
                nc.vector.tensor_copy(state[:, 0, :], TU[:, 0:P]).then_inc(s("state_step"), 1)
                for c in range(1, NC - 1):
                    dve.wait_ge(s("state_step"), (NC - 2) * (n - 1) + c)
                    nc.vector.scalar_tensor_tensor(
                        out=state[:, c, :], in0=state[:, c - 1, :], scalar=cst[:, jp % 2, CST - 1:CST],
                        in1=TU[:, c * P:(c + 1) * P], op0=ALU.mult, op1=ALU.add
                    ).then_inc(s("state_step" if c < NC - 2 else "state_done"), 1)

            def gate(n, jp, pairs):
                nwcol = nw_half[:, n - 1:n] if isinstance(n, int) else nw_half[:, bass.ds(n - 1, 1)]
                dve.wait_ge(s("gate_ready"), n)
                dve.wait_ge(s("squared"), n)
                nc.vector.scalar_tensor_tensor(out=gt[:, :], in0=th[:, :], scalar=1.0, in1=SC,
                                               op0=ALU.add, op1=ALU.mult).then_inc(s("gated"), 1)
                dve.wait_ge(s("sq_added"), n - 1)
                nc.vector.tensor_tensor(sq_sum[:, :], sq_sum[:, :], sq[:, :], ALU.add).then_inc(s("sq_added"), 1)
                dve.wait_ge(s("gated"), n)
                if jp % 2 == 0:
                    dve.wait_ge(s("out_done"), 4 * pairs)
                nc.vector.tensor_scalar(g_h[:, jp % 2, :], gt[:, :], nwcol, None, ALU.mult).then_inc(s("g_hi"), 1)
                dve.wait_ge(s("g_hi"), n)
                nc.vector.scalar_tensor_tensor(out=g_l[:, jp % 2, :], in0=gt[:, :], scalar=nwcol,
                                               in1=g_h[:, jp % 2, :], op0=ALU.mult, op1=ALU.subtract
                                               ).then_inc(s("g_ready"), 1)

            def add_out(pair):
                dve.wait_ge(s("out_added"), 4 * pair)
                for i in range(4):
                    dve.wait_ge(s("out_done"), 4 * pair + i + 1)
                    a = acc[:, 2 * i:2 * i + 2, :].rearrange("p a b -> p (a b)")
                    nc.vector.tensor_tensor(a, a, UNIT[(i + 1) % 2], ALU.add).then_inc(s("out_added"), 1)

            def step(g, j, first):
                n = g * G4 + j
                jp = (j - 1) % G4
                if not first:
                    states(n, jp)
                    gate(n, jp, 2 * g + jp // 2)
                dve.wait_ge(s("q_ready"), n + 1)
                dve.wait_ge(s(f"cst_in{j % 2}"), 32 * g + 16 * (j // 2) + 16)
                nc.vector.tensor_tensor(heads_of(qdT[:, :]), heads_of(qT[:, :]),
                                        cst[:, j % 2:j % 2 + 1, P:2 * P].to_broadcast([P, NC, P]), ALU.mult
                                        ).then_inc(s("q_decayed"), 1)
                if j == 2 or (j == 0 and not first):
                    add_out(2 * g - (j == 0))
                dve.wait_ge(s("keys_turned"), n + 1)
                nc.vector.tensor_scalar(k_nat[:, :, :].rearrange("p c d -> p (c d)"), TU,
                                        cst[:, j % 2, 2 * P:2 * P + 1], None, ALU.mult
                                        ).then_inc(s("k_nat_ready"), 1)
                dve.wait_ge(s("scores_done"), n + 1)
                nc.vector.tensor_tensor(sd[:, :, :], heads_of(SC),
                                        cst[:, j % 2:j % 2 + 1, 0:P].to_broadcast([P, NC, P]), ALU.mult
                                        ).then_inc(s("sd_ready"), 1)

            for j in range(G4):
                step(0, j, j == 0)
            with dve.Fori(1, NG) as g:
                for j in range(G4):
                    step(g, j, False)
            states(H0, G4 - 1)
            gate(H0, G4 - 1, None)
            add_out(2 * NG - 1)
            dve.wait_ge(s("sq_summed"), 1)
            nc.vector.tensor_scalar(ms[:, :], SC[:, 0:NT], 1.0 / (H0 * DH0), EPS, ALU.mult, ALU.add
                                    ).then_inc(s("ms_ready"), 1)
            dve.wait_ge(s("rms_ready"), 1)
            dve.wait_ge(s("out_added"), 8 * NG)
            dve.wait_ge(s("x_again_in"), 16)
            for t in range(NT):
                nc.vector.scalar_tensor_tensor(out=x[:, t, :], in0=acc[:, t, :], scalar=rms[:, t:t + 1],
                                               in1=x_again[:, t, :], op0=ALU.mult, op1=ALU.add).then_inc(s("x_out"), 1)
            dve.wait_ge(s("x_out"), NT)

        @block.tensor
        def _(pe):
            pe.wait_ge(s("ident_in"), 16)
            def project(unit, j, c0, first=False):
                for half in range(2):
                    if first:
                        ln_tensor(nc, pe, s, b, range(4 * half, 4 * half + 4))
                        pe.wait_ge(s("ln_lo"), 4 * half + 4)
                        pe.wait_ge(s("w_ready"), 1)
                    q = slice(half * BANK, (half + 1) * BANK)
                    for k in range(KT):
                        w = slice(c0 + k * P, c0 + (k + 1) * P)
                        last = mm3(nc, UNIT[unit][:, q], w_h[:, j, w], w_l[:, j, w], xh_h[:, k, q], xh_l[:, k, q],
                                   k == 0, k == KT - 1)
                last.then_inc(s("proj_done"), 1)

            def project_v(i):
                for a in range(2):
                    t = slice((2 * i + a) * P, (2 * i + a + 1) * P)
                    out = UNIT[i % 2][:, a * BANK:(a + 1) * BANK]
                    for k in range(KT):
                        last = mm3(nc, out, xh_h[:, k, t], xh_l[:, k, t], w_h[:, k, 3 * 512:], w_l[:, k, 3 * 512:],
                                   k == 0, k == KT - 1)
                last.then_inc(s("proj_done"), 1)

            def output(i):
                for a in range(2):
                    t = slice((2 * i + a) * P, (2 * i + a + 1) * P)
                    out = UNIT[(i + 1) % 2][:, a * BANK:(a + 1) * BANK]
                    for h in range(2):
                        last = mm3(nc, out, g_h[:, h, t], g_l[:, h, t], o_h[:, h, :], o_l[:, h, :],
                                   h == 0, h == 1)
                last.then_inc(s("out_done"), 1)

            def output_pair(p, n, bank1, value):
                pe.wait_ge(s("g_ready"), 2 * p + 2)
                pe.wait_ge(s("o_ready"), 2 * p + 2)
                pe.wait_ge(s(bank1), value)
                output(0)
                pe.wait_ge(s("gate_ready"), n + 1)
                output(1)
                pe.wait_ge(s("out_added"), 4 * p + 1)
                output(2)
                pe.wait_ge(s("out_added"), 4 * p + 2)
                output(3)

            def update(n, jp):
                pe.wait_ge(s("k_nat_ready"), n)
                for c in range(NC - 1):
                    last = nc.tensor.matmul(TU[:, c * P:(c + 1) * P], k_nat[:, c, :],
                                            v_nat[:, c, jp * DH0:(jp + 1) * DH0], start=True, stop=True)
                last.then_inc(s("updates_done"), 1)

            def attend(n, jp):
                pe.wait_ge(s("sd_ready"), n)
                pe.wait_ge(s("q_decayed"), n)
                pe.wait_ge(s("state_done"), n)
                for c in range(NC):
                    q = slice(c * P, (c + 1) * P)
                    last = nc.tensor.matmul(SC[:, q], v_nat[:, c, jp * DH0:(jp + 1) * DH0], sd[:, c, :],
                                            start=True, stop=c == 0)
                    if c:
                        last = nc.tensor.matmul(SC[:, q], state[:, c - 1, :], qdT[:, q], start=False, stop=True)
                last.then_inc(s("attn_done"), 1)

            def score(n, first):
                pe.wait_ge(s("k_ready"), n + 1)
                if not first:
                    pe.wait_ge(s("state_done"), n)
                for c in range(NC):
                    q = slice(c * P, (c + 1) * P)
                    last = nc.tensor.transpose(TU[:, q], kT[:, q], ident[:, :])
                last.then_inc(s("keys_turned"), 1)
                if not first:
                    pe.wait_ge(s("gated"), n)
                for c in range(NC):
                    q = slice(c * P, (c + 1) * P)
                    last = nc.tensor.matmul(SC[:, q], kT[:, q], qT[:, q], start=True, stop=True)
                last.then_inc(s("scores_done"), 1)

            def step(g, j, first, group0):
                n = g * G4 + j
                jp = (j - 1) % G4
                if not first:
                    pe.wait_ge(s("w_ready"), n + 1)
                if not first:
                    if j in (0, 2):
                        pe.wait_ge(s("k_ready"), n)
                    elif j == 1 and group0:
                        pe.wait_ge(s("v_ready"), 4)
                    else:
                        pe.wait_ge(s("out_added"), 8 * g + (-1 if j == 1 else 3))
                project(Q_UNIT[j], j, 0, first)
                if not first:
                    update(n, jp)
                    if j in (0, 2) or (j == 1 and group0):
                        pe.wait_ge(s("gate_ready"), n)
                    else:
                        pe.wait_ge(s("out_added"), 8 * g + (0 if j == 1 else 4))
                project(K_UNIT[j], j, 512)
                if not first:
                    attend(n, jp)
                if j == 0:
                    pe.wait_ge(s("w_ready"), n + G4)
                    pe.wait_ge(s("q_ready"), n + 1)
                    project_v(0)
                    pe.wait_ge(s("k_ready"), n + 1)
                    project_v(1)
                    pe.wait_ge(s("v_ready"), n + 1)
                    project_v(2)
                    pe.wait_ge(s("v_ready"), n + 2)
                    project_v(3)
                    pe.wait_ge(s("v_ready"), n + 3)
                else:
                    pe.wait_ge(s("q_ready"), n + 1)
                project(G_UNIT[j], j, 1024)
                if j == 0 and not first:
                    output_pair(2 * g - 1, n, "v_ready", n + 4)
                if j == 2:
                    output_pair(2 * g, n, "k_ready", n + 1)
                score(n, first)

            for j in range(G4):
                step(0, j, j == 0, True)
            with pe.Fori(1, NG) as g:
                for j in range(G4):
                    step(g, j, False, False)
            update(H0, G4 - 1)
            attend(H0, G4 - 1)
            output_pair(2 * NG - 1, H0 - 1, "gate_ready", H0)
            pe.wait_ge(s("sq_added"), H0)
            pe.wait_ge(s("gated"), H0)
            for t in range(NT):
                last = nc.tensor.matmul(SC[:, t:t + 1], sq_sum[:, t * P:(t + 1) * P], ones[:, :],
                                        start=True, stop=True)
            last.then_inc(s("sq_summed"), 1)


def stage_ffn0(nc, top, w1_dram, w3_dram, w2_dram, lora_a_dram, lora_b2_dram):
    ctx = ExitStack()
    with ctx:
        def sb(name, shape, dt=F32):
            return ctx.enter_context(nc.sbuf_tensor(f"f0_{name}", shape, dt))
        s = Sems(nc, ctx, "f0")
        ps = ctx.enter_context(nc.psum_tensor("f0_ps", [P, 8, BANK], F32))
        H1, H3, DELTA, OUT = ps[:, 0, :], ps[:, 1, :], ps[:, 2, :], 4
        xh_h, xh_l = sb("xh_h", [P, KT, T], F32R), sb("xh_l", [P, KT, T], F32R)
        WC = 512 + P
        raw = {w: sb(f"raw{w}", [P, WC]) for w in (1, 3, 2)}
        w_h = {w: sb(f"w{w}_h", [P, WC], F32R) for w in (1, 3, 2)}
        w_l = {w: sb(f"w{w}_l", [P, 512], F32R) for w in (1, 3, 2)}
        w2m = sb("w2m", [P, D])
        la = sb("la", [P, 2, KT, LR])
        la_h, la_l = sb("la_h", [P, 2, KT, LR], F32R), sb("la_l", [P, 2, KT, LR], F32R)
        b2 = sb("b2", [LR, D])
        b2_st = sb("b2_st", [LR, D], F32R)
        low = sb("low", [LR, 2, T])
        low_st = sb("low_st", [LR, 2, T], F32R)
        silu = sb("silu", [P, BANK])
        g = sb("g", [P, BANK])
        g_h, g_l = sb("g_h", [P, BANK], F32R), sb("g_l", [P, BANK], F32R)
        x = top["x"]
        b = dict(top, ps=ps, xh_h=xh_h, xh_l=xh_l, xn=sb("xn", [P, 2, D]))
        block = ctx.enter_context(nc.Block())
        LO = slice(32, 64)
        LO_S = slice(64, 96)
        flat = lambda ap: ap.rearrange("p a b -> p (a b)")
        w_dram = {1: w1_dram, 3: w3_dram, 2: w2_dram}
        FREED = {1: "w1_split", 3: "w3_split", 2: "w2_merged"}

        @block.sync
        def _(sp):
            sp.dma_start(la[:, :, :, :], lora_a_dram).then_inc(s("la_in"), 16)
            sp.dma_start(b2[:, :], lora_b2_dram).then_inc(s("b2_in"), 16)

            def load(w, f, step):
                sp.wait_ge(s(FREED[w]), step)
                sp.dma_start(raw[w][:, :], w_dram[w][f]).then_inc(s(f"raw{w}_in"), 16)

            for half in range(2):
                for w in (1, 2, 3):
                    load(w, 0, half * NF0)
                with sp.Fori(1, NF0) as f:
                    for w in (1, 2, 3):
                        load(w, f, f + half * NF0)

        @block.gpsimd
        def _(pool):
            for t in range(4):
                ln_gpsimd(nc, pool, s, b, t)
            pool.wait_ge(s("la_in"), 16)
            split_hi(nc.gpsimd, la_h[:, :, :, :].rearrange("p a b c -> p (a b c)"),
                     la[:, :, :, :].rearrange("p a b c -> p (a b c)")).then_inc(s("la_hi"), 1)
            pool.wait_ge(s("la_hi"), 1)
            nc.gpsimd.tensor_tensor(la_l[:, :, :, :].rearrange("p a b c -> p (a b c)"),
                                    la[:, :, :, :].rearrange("p a b c -> p (a b c)"),
                                    la_h[:, :, :, :].rearrange("p a b c -> p (a b c)"), ALU.subtract
                                    ).then_inc(s("la_split"), 1)
            pool.wait_ge(s("b2_in"), 16)
            split_hi(nc.gpsimd, b2_st[:, :], b2[:, :]).then_inc(s("b2_hi"), 1)
            pool.wait_ge(s("b2_hi"), 1)
            nc.gpsimd.tensor_tensor(b2_st[LO, :], b2[LO, :], b2_st[LO, :], ALU.subtract).then_inc(s("b2_split"), 1)
            pool.wait_ge(s("b2_split"), 1)

            def split(w, step):
                pool.wait_ge(s(f"raw{w}_in"), 16 * step + 16)
                pool.wait_ge(s(f"h{w}_done"), step)
                take_wait(nc, top, step)
                split_hi(nc.gpsimd, w_h[w][:, :], raw[w][:, :]).then_inc(s(f"w{w}_hi"), 1)
                pool.wait_ge(s(f"w{w}_hi"), step + 1)
                nc.gpsimd.tensor_tensor(w_h[w][LO_S, 512:WC], raw[w][LO_S, 512:WC], w_h[w][LO_S, 512:WC],
                                        ALU.subtract).then_inc(s(f"w{w}_lora"), 1)
                pool.wait_ge(s(f"w{w}_lora"), step + 1)
                nc.gpsimd.tensor_tensor(w_l[w][:, :], raw[w][:, 0:512], w_h[w][:, 0:512], ALU.subtract
                                        ).then_inc(s(f"w{w}_split"), 1)

            def split_a2(step):
                pool.wait_ge(s("raw2_in"), 16 * step + 16)
                pool.wait_ge(s("delta_done"), step)
                take_wait(nc, top, step)
                split_hi(nc.gpsimd, w_h[2][:, 512:WC], raw[2][:, 512:WC]).then_inc(s("a2_hi"), 1)
                pool.wait_ge(s("a2_hi"), step + 1)
                nc.gpsimd.tensor_tensor(w_h[2][LO_S, 512:WC], raw[2][LO_S, 512:WC], w_h[2][LO_S, 512:WC],
                                        ALU.subtract).then_inc(s("a2_split"), 1)
                pool.wait_ge(s("a2_split"), step + 1)

            def split_w2(step):
                pool.wait_ge(s("w2_merged"), step + 1)
                pool.wait_ge(s("out_step"), step)
                take_wait(nc, top, step)
                split_hi(nc.gpsimd, w_h[2][:, 0:512], w2m[:, :]).then_inc(s("w2_hi"), 1)
                pool.wait_ge(s("w2_hi"), step + 1)
                nc.gpsimd.tensor_tensor(w_l[2][:, :], w2m[:, :], w_h[2][:, 0:512], ALU.subtract
                                        ).then_inc(s("w2_split"), 1)

            for t in range(4, NT):
                ln_gpsimd(nc, pool, s, b, t)
            split(1, 0)
            split(3, 0)
            def turn(step):
                split_a2(step)
                split(1, step + 1)
                split_w2(step)
                split(3, step + 1)

            turn(0)
            with pool.Fori(1, 2 * NF0 - 1) as step:
                turn(step)
            split_a2(2 * NF0 - 1)
            split_w2(2 * NF0 - 1)

        @block.scalar
        def _(act):
            ln_scalar(nc, act, s, b)
            for i in range(2):
                act.wait_ge(s("low_done"), i + 1)
                nc.scalar.activation(low[:, i, :], flat(ps[0:LR, 2 * i:2 * i + 2, :]), ACT.Copy, scale=LORA_SCALE
                                     ).then_inc(s("low_ready"), 1)

            def gate(step):
                act.wait_ge(s("h1_done"), step + 1)
                act.wait_ge(s("g_made"), step)
                nc.scalar.activation(silu[:, :], H1, ACT.Silu).then_inc(s("silu_ready"), 1)

            gate(0)
            with act.Fori(1, 2 * NF0) as step:
                gate(step)

        @block.vector
        def _(dve):
            ln_vector(nc, dve, s, b)
            for i in range(2):
                dve.wait_ge(s("low_ready"), i + 1)
                nc.vector.tensor_copy(low_st[:, i, :], low[:, i, :]).then_inc(s("low_hi"), 1)
                dve.wait_ge(s("low_hi"), i + 1)
                nc.vector.tensor_tensor(low_st[LO, i, :], low[LO, i, :], low_st[LO, i, :], ALU.subtract
                                        ).then_inc(s("low_split"), 1)

            def merge(step):
                dve.wait_ge(s("delta_done"), step + 1)
                dve.wait_ge(s("raw2_in"), 16 * step + 16)
                dve.wait_ge(s("w2_split"), step)
                nc.vector.scalar_tensor_tensor(out=w2m[:, :], in0=DELTA, scalar=LORA_SCALE, in1=raw[2][:, 0:512],
                                               op0=ALU.mult, op1=ALU.add).then_inc(s("w2_merged"), 1)

            def product(step):
                dve.wait_ge(s("silu_ready"), step + 1)
                dve.wait_ge(s("h3_done"), step + 1)
                dve.wait_ge(s("g_split"), step)
                nc.vector.tensor_tensor(g[:, :], silu[:, :], H3, ALU.mult).then_inc(s("g_made"), 1)
                dve.wait_ge(s("g_made"), step + 1)
                nc.vector.tensor_copy(g_h[:, :], g[:, :]).then_inc(s("g_hi"), 1)
                dve.wait_ge(s("g_hi"), step + 1)
                nc.vector.tensor_tensor(g_l[:, :], g[:, :], g_h[:, :], ALU.subtract).then_inc(s("g_split"), 1)

            for half in range(2):
                merge(half * NF0)
                product(half * NF0)
                with dve.Fori(1, NF0) as f:
                    merge(f + half * NF0)
                    product(f + half * NF0)
                dve.wait_ge(s("out_step"), (half + 1) * NF0)
                for i in range(4):
                    t = 4 * half + i
                    nc.vector.tensor_tensor(x[:, t, :], x[:, t, :], ps[:, OUT + i, :], ALU.add
                                            ).then_inc(s("out_added"), 1)
            dve.wait_ge(s("out_added"), NT)

        @block.tensor
        def _(pe):
            for half in range(2):
                ln_tensor(nc, pe, s, b, range(4 * half, 4 * half + 4))
                pe.wait_ge(s("la_split"), 1)
                pe.wait_ge(s("ln_lo"), 4 * half + 4)
                q = slice(half * BANK, (half + 1) * BANK)
                for i in range(2):
                    for k in range(KT):
                        last = mm3(nc, ps[0:LR, 2 * i + half, :], la_h[:, i, k, :], la_l[:, i, k, :],
                                   xh_h[:, k, q], xh_l[:, k, q], k == 0, k == KT - 1)
                    if half:
                        last.then_inc(s("low_done"), 1)
            pe.wait_ge(s("low_split"), 2)
            pe.wait_ge(s("b2_split"), 1)

            def hidden(w, bank, half):
                q = slice(half * BANK, (half + 1) * BANK)
                for k in range(KT):
                    c = slice(k * P, (k + 1) * P)
                    mm3(nc, bank, w_h[w][:, c], w_l[w][:, c], xh_h[:, k, q], xh_l[:, k, q], k == 0, False)
                nc.tensor.matmul(bank, w_h[w][0:LR, 512:WC], low_st[:, (w - 1) // 2, q], start=False, stop=True
                                 ).then_inc(s(f"h{w}_done"), 1)

            def out(start, stop, step):
                pe.wait_ge(s("g_split"), step)
                pe.wait_ge(s("w2_split"), step)
                for i in range(4):
                    t = slice(i * P, (i + 1) * P)
                    last = mm3(nc, ps[:, OUT + i, :], g_h[:, t], g_l[:, t], w_h[2][:, 0:512], w_l[2][:, :],
                               start, stop)
                last.then_inc(s("out_step"), 1)

            def step(n, half, out_start, out_stop):
                pe.wait_ge(s("w1_split"), n + 1)
                pe.wait_ge(s("silu_ready"), n)
                hidden(1, H1, half)
                if out_start is not None:
                    out(out_start, out_stop, n)
                pe.wait_ge(s("a2_split"), n + 1)
                pe.wait_ge(s("w2_merged"), n)
                nc.tensor.matmul(DELTA, w_h[2][0:LR, 512:WC], b2_st[:, :], start=True, stop=True
                                 ).then_inc(s("delta_done"), 1)
                pe.wait_ge(s("w3_split"), n + 1)
                pe.wait_ge(s("g_made"), n)
                hidden(3, H3, half)

            for half in range(2):
                n0 = half * NF0
                step(n0, half, False if half else None, True)
                if half:
                    pe.wait_ge(s("out_added"), 4)
                step(n0 + 1, half, True, False)
                with pe.Fori(2, NF0) as f:
                    step(f + n0, half, False, False)
            out(False, True, 2 * NF0)


def stage_attention1(nc, top, a):
    ctx = ExitStack()
    with ctx:
        def sb(name, shape, dt=F32):
            return ctx.enter_context(nc.sbuf_tensor(f"a1_{name}", shape, dt))
        q2 = sb("q2", [P, NT, H1 * 2 * DH1])
        k2 = sb("k2", [P, NT, H1 * 2 * DH1])
        v1 = sb("v1", [P, NT, H1, DH1 + 1])
        attention1_qkv(nc, top, q2, k2, v1, a["a1_wqkv"], a["a1_ln"])
        attn = sb("attn", [P, NT, D])
        attention1_heads(nc, top, q2, k2, v1, attn, a)
        attention1_out(nc, top, attn, a["a1_wout"])


def attention1_qkv(nc, top, q2, k2, v1, w_dram, ln_dram):
    ctx = ExitStack()
    with ctx:
        def sb(name, shape, dt=F32):
            return ctx.enter_context(nc.sbuf_tensor(f"a1q_{name}", shape, dt))
        s = Sems(nc, ctx, "a1q")
        ps = ctx.enter_context(nc.psum_tensor("a1q_ps", [P, 8, BANK], F32))
        xh_h, xh_l = sb("xh_h", [P, KT, T], F32R), sb("xh_l", [P, KT, T], F32R)
        raw = sb("raw", [P, KT * D])
        w_h, w_l = sb("w_h", [P, 2, KT * D], F32R), sb("w_l", [P, 2, KT * D], F32R)
        wb = sb("wb", [P, 4, D])
        R = 4
        cl = sb("cl", [P, R, D])
        st, mv = sb("st", [P, R, 6]), sb("mv", [P, R, 2])
        ve, rs, sh = sb("ve", [P, R]), sb("rs", [P, R]), sb("sh", [P, R])
        b = dict(top, ps=ps, xh_h=xh_h, xh_l=xh_l, xn=sb("xn", [P, 2, D]))
        block = ctx.enter_context(nc.Block())
        QK = 2 * NT

        def half(m, which):
            dst = (q2, k2)[m // NT]
            return dst[:, m % NT, :].rearrange("p (h w d) -> p h w d", h=H1, w=2)[:, :, which, :]

        by_head = lambda ap: ap.rearrange("p (h d) -> p h d", h=H1)

        @block.sync
        def _(sp):
            for c in range(3):
                if c:
                    sp.wait_ge(s("w_split"), c)
                sp.dma_start(raw[:, :], w_dram[c]).then_inc(s("raw_in"), 16)
                if c == 0:
                    for i in range(4):
                        sp.dma_start(wb[:, i, :], ln_dram[i:i + 1, :].to_broadcast([P, D])).then_inc(s("wb_in"), 16)

        @block.gpsimd
        def _(pool):
            def split(c):
                pool.wait_ge(s("raw_in"), 16 * c + 16)
                split_hi(nc.gpsimd, w_h[:, c % 2, :], raw[:, :]).then_inc(s("w_hi"), 1)
                pool.wait_ge(s("w_hi"), c + 1)
                nc.gpsimd.tensor_tensor(w_l[:, c % 2, :], raw[:, :], w_h[:, c % 2, :], ALU.subtract
                                        ).then_inc(s("w_split"), 1)

            def moments(m):
                r = slice(m % R, m % R + 1)
                pool.wait_ge(s("stats"), m + 1)
                nc.gpsimd.tensor_scalar(ve[:, r], mv[:, m % R, 1:2], 1.0, EPS, ALU.mult, ALU.add).then_inc(s("ve"), 1)
                pool.wait_ge(s("ve"), m + 1)
                nc.gpsimd.tensor_tensor(rs[:, r], ve[:, r], top["neg_half"][:, 0:1], ALU.pow).then_inc(s("rs"), 1)
                pool.wait_ge(s("rs"), m + 1)
                nc.gpsimd.tensor_scalar(sh[:, r], mv[:, m % R, 0:1], rs[:, r], -1.0, ALU.mult, ALU.mult
                                        ).then_inc(s("sh"), 1)

            def scale(m):
                pool.wait_ge(s("normed"), m + 1)
                nc.gpsimd.tensor_tensor(cl[:, m % R, :], cl[:, m % R, :], wb[:, 2 * (m // NT), :], ALU.mult
                                        ).then_inc(s("scaled"), 1)

            for t in range(NT):
                ln_gpsimd(nc, pool, s, b, t)
                if t == 1:
                    split(0)
            split(1)
            pool.wait_ge(s("wb_in"), 64)
            for m in range(QK + 1):
                if m < QK:
                    moments(m)
                if m >= 1:
                    scale(m - 1)
                if m == NT:
                    pool.wait_ge(s("proj_done"), NT)
                    split(2)

        @block.scalar
        def _(act):
            ln_scalar(nc, act, s, b)
            for m in range(QK + 2):
                r = m % R
                if m < QK:
                    act.wait_ge(s("sh"), m + 1)
                    nc.scalar.activation(cl[:, r, :], cl[:, r, :], ACT.Identity, bias=sh[:, r:r + 1],
                                         scale=rs[:, r:r + 1]).then_inc(s("normed"), 1)
                if m >= 2:
                    act.wait_ge(s("shifted"), m - 1)
                    nc.scalar.copy(half(m - 2, 0).bitcast(F32R), by_head(cl[:, (m - 2) % R, :])).then_inc(s("hi"), 1)

        @block.vector
        def _(dve):
            nc.vector.memset(v1[:, :, :, DH1:DH1 + 1], 1.0).then_inc(s("ones"), 1)
            ln_vector(nc, dve, s, b)

            dve.wait_ge(s("wb_in"), 64)

            def shift(m):
                dve.wait_ge(s("scaled"), m + 1)
                nc.vector.tensor_tensor(cl[:, m % R, :], cl[:, m % R, :], wb[:, 2 * (m // NT) + 1, :], ALU.add
                                        ).then_inc(s("shifted"), 1)

            def low_half(m):
                dve.wait_ge(s("hi"), m + 1)
                nc.vector.tensor_tensor(half(m, 1).bitcast(F32R), by_head(cl[:, m % R, :]), half(m, 0),
                                        ALU.subtract).then_inc(s("lo"), 1)

            for m in range(3 * NT):
                r = m % R
                dve.wait_ge(s("proj_done"), m + 1)
                if m < QK:
                    if m >= R:
                        dve.wait_ge(s("lo"), m - R + 1)
                    nc.vector.tensor_scalar(cl[:, r, :], ps[:, m % 8, :], CLIP, -CLIP, ALU.min, ALU.max
                                            ).then_inc(s("clipped"), 1)
                    dve.wait_ge(s("clipped"), m + 1)
                    nc.vector.bn_stats(st[:, r, :], cl[:, r, :]).then_inc(s("st"), 1)
                    dve.wait_ge(s("st"), m + 1)
                    nc.vector.bn_aggr(mv[:, r, :], st[:, r, :]).then_inc(s("stats"), 1)
                else:
                    nc.vector.tensor_scalar(v1[:, m % NT, :, 0:DH1], by_head(ps[:, m % 8, :]), CLIP, -CLIP,
                                            ALU.min, ALU.max).then_inc(s("clipped"), 1)
                if 2 <= m < QK + 2:
                    shift(m - 2)
                if 3 <= m < QK + 3:
                    low_half(m - 3)
            dve.wait_ge(s("lo"), QK)
            dve.wait_ge(s("clipped"), 3 * NT)
            dve.wait_ge(s("ones"), 1)

        @block.tensor
        def _(pe):
            ln_tensor(nc, pe, s, b, range(2))
            for m in range(3 * NT):
                if m < NT:
                    ln_tensor(nc, pe, s, b, range(m + 2, min(m + 3, NT)))
                    pe.wait_ge(s("ln_lo"), m + 1)
                c, t = m // NT, slice((m % NT) * P, (m % NT + 1) * P)
                pe.wait_ge(s("w_split"), c + 1)
                if m >= 8:
                    pe.wait_ge(s("clipped"), m - 7)
                for k in range(KT):
                    w = slice(k * D, (k + 1) * D)
                    last = mm3(nc, ps[:, m % 8, :], xh_h[:, k, t], xh_l[:, k, t], w_h[:, c % 2, w], w_l[:, c % 2, w],
                               k == 0, k == KT - 1)
                last.then_inc(s("proj_done"), 1)


QROW = 4 * DH1
MAXROW = QROW + 2 * NT
ROWS = 96
BIG = 1e30


def attention1_heads(nc, top, q2, k2, v1, attn, a):
    ctx = ExitStack()
    with ctx:
        def sb(name, shape, dt=F32):
            return ctx.enter_context(nc.sbuf_tensor(f"a1h_{name}", shape, dt))
        s = Sems(nc, ctx, "a1h")
        ps = ctx.enter_context(nc.psum_tensor("a1h_ps", [P, 8, BANK], F32))
        two = lambda i: ps[:, i:i + 2, :].rearrange("p a b -> p (a b)")
        S = [two(0), two(2)]
        M = [ps[:, 4, :], ps[:, 5, :]]
        R = [ps[:, 0, :], ps[:, 2, :]]
        O = two(6)
        V1 = DH1 + 1
        qs, ks = sb("qs", [P, NT, 4, 2, DH1]), sb("ks", [P, NT, 2, 2, 2 * DH1])
        vs = sb("vs", [P, 2, NT, 2 * V1])
        QT = [sb(f"QT{i}", [ROWS, T], F32R) for i in range(4)]
        KTs = [sb(f"KT{i}", [ROWS, T], F32R) for i in range(4)]
        pr = [[sb(f"pr{b}{kt}", [P, T - kt * P]) for kt in range(NT)] for b in range(2)]
        aug = sb("aug", [ROWS, 2, T])
        slope = sb("slope", [ROWS, H1])
        maskf, mask = sb("maskf", [P, 2, P]), sb("mask", [P, 2, P], BF16)
        identb = sb("identb", [P, P], BF16)
        mx2, mx = sb("mx2", [P, NT, 2]), sb("mx", [P, 2, NT])
        crow = sb("crow", [NT, 2, P], F32R)
        osb = sb("osb", [P, T])
        orow = sb("orow", [P, NT, V1])
        rsum = sb("rsum", [P, NT, 1])
        ident = top["ident"]
        block = ctx.enter_context(nc.Block())
        AUG = slice(QROW, ROWS)
        GROUPS = H1 // 4
        PIECES = [(t, 0, (t + 1) * P) for t in range(4)]
        for t in range(4, NT):
            PIECES += [(t, 0, BANK), (t, 1, (t - 3) * P)]
        NP = len(PIECES)
        mbank = lambda k: M[1 - k % 2]

        def at(i, w):
            return slice(i * w, (i + 1) * w) if isinstance(i, int) else bass.ds(i * w, w)

        def gather_pair(engine, p):
            src = q2[:, :, at(p, 64)].rearrange("p t (a d) -> p t a d", d=DH1)
            for rep in range(2):
                engine.tensor_copy(qs[:, :, :, rep, :], src).then_inc(s("gathered"), 1)
            src = k2[:, :, at(p, 64)].rearrange("p t (a d) -> p t a d", d=2 * DH1)
            for rep in range(2):
                engine.tensor_copy(ks[:, :, :, rep, :], src).then_inc(s("gathered"), 1)

        @block.sync
        def _(sp):
            sp.dma_start(aug[AUG, :, :], a["a1_aug"]).then_inc(s("const_in"), 16)
            sp.dma_start(slope[AUG, :], a["a1_slope"]).then_inc(s("const_in"), 16)
            sp.dma_start(maskf[:, :, :], a["a1_mask"]).then_inc(s("const_in"), 16)

            def max_row(i, e):
                sp.wait_ge(s("crow_ready"), i + 1)
                sp.dma_start(QT[e][MAXROW:MAXROW + 1, :].bitcast(F32).rearrange("o (t q) -> o t q", t=NT),
                             crow[:, e % 2, :].bitcast(F32)).then_inc(s(f"max_in{e % 2}"), 16)

            with sp.Fori(0, GROUPS) as g:
                for e in range(4):
                    max_row(4 * g + e, e)

        @block.gpsimd
        def _(pool):
            pool.wait_ge(s("const_in"), 48)

            def gather(p, pp, first, second):
                if not first:
                    pool.wait_ge(s("turned"), 2 * p)
                if not first:
                    gather_pair(nc.gpsimd, p)
                if not (first or second):
                    pool.wait_ge(s("scored"), 8 * (2 * p - 2))
                for h in range(2):
                    if not first:
                        pool.wait_ge(s("gathered"), 4 * p + 4)
                    nc.gpsimd.tensor_tensor(QT[2 * pp + h][AUG, :], aug[AUG, 1, :],
                                            slope[AUG, at(2 * p + h, 1)].to_broadcast([ROWS - QROW, T]), ALU.mult
                                            ).then_inc(s("qaug"), 1)
                    pool.wait_ge(s("qaug"), 2 * p + h + 1)
                if not (first or second):
                    pool.wait_ge(s("values_done"), 2 * p - 2)
                nc.gpsimd.tensor_copy(vs[:, pp, :, :],
                                      v1[:, :, :, :].rearrange("p t h d -> p t (h d)")[:, :, at(p, 2 * V1)]
                                      ).then_inc(s("v_gathered"), 1)

            gather(0, 0, True, False)
            gather(1, 1, False, True)
            with pool.Fori(1, GROUPS) as g:
                for pp in range(2):
                    gather(2 * g + pp, pp, False, False)

        @block.scalar
        def _(act):
            act.wait_ge(s("const_in"), 48)
            nc.scalar.copy(KTs[0][AUG, :], aug[AUG, 0, :]).then_inc(s("act_const"), 1)
            nc.scalar.copy(mask[:, :, :], maskf[:, :, :]).then_inc(s("act_const"), 1)
            nc.scalar.copy(identb[:, :], ident[:, :]).then_inc(s("act_const"), 1)

            def stacks(pairs, e):
                act.wait_ge(s("turned"), 2 * pairs + 1)
                nc.scalar.copy(QT[e][0:QROW, :], S[0][0:QROW, :]).then_inc(s("stacks_first"), 1)
                act.wait_ge(s("turned"), 2 * pairs + 2)
                nc.scalar.copy(KTs[e][0:QROW, :], S[1][0:QROW, :]).then_inc(s("stacks_first"), 1)

            def exp(i, e, kt):
                act.wait_ge(s("scored"), 8 * i + kt + 1)
                if kt == 0 and not (isinstance(i, int) and i < 2):
                    act.wait_ge(s("values_done"), i - 1)
                nc.scalar.activation(pr[e % 2][kt][:, :], S[kt % 2][:, kt * P:T], ACT.Exp, scale=0.25
                                     ).then_inc(s("exp_done"), 1)

            def take_output(i):
                act.wait_ge(s("values_done"), i)
                if not (isinstance(i, int) and i < 2):
                    act.wait_ge(s("rows_done"), 2 * i - 2)
                nc.scalar.copy(osb[:, :], O).then_inc(s("o_taken"), 1)

            def step(i, e, pair=None, first=False):
                if pair is not None:
                    stacks(pair, (e + 2) % 4)
                for kt in range(NT):
                    exp(i, e, kt)
                    if kt == 3 and not first:
                        take_output(i)

            nc.scalar.copy(KTs[1][AUG, :], aug[AUG, 0, :]).then_inc(s("act_const"), 1)
            stacks(0, 0)
            for e in (2, 3):
                nc.scalar.copy(KTs[e][AUG, :], aug[AUG, 0, :]).then_inc(s("act_const"), 1)
            for e in range(4):
                step(e, e, 1 + e // 2 if e % 2 == 0 else None, e == 0)
            with act.Fori(1, GROUPS - 1) as g:
                for e in range(4):
                    step(4 * g + e, e, 2 * g + 1 + e // 2 if e % 2 == 0 else None)
            for e in range(4):
                step(H1 - 4 + e, e, H1 // 2 - 1 if e == 0 else None)
            take_output(H1)

        @block.vector
        def _(dve):
            gather_pair(nc.vector, 0)
            nc.vector.memset(O, 0.0).then_inc(s("o_clear"), 1)
            nc.vector.memset(mx2[:, :, :], BIG).then_inc(s("mx2_clear"), 1)
            dve.wait_ge(s("mx2_clear"), 1)

            def stacks(pairs, e):
                dve.wait_ge(s("turned"), 2 * pairs + 1)
                nc.vector.tensor_copy(QT[e + 1][0:QROW, :], S[0][QROW:2 * QROW, :]).then_inc(s("stacks_second"), 1)
                dve.wait_ge(s("turned"), 2 * pairs + 2)
                nc.vector.tensor_copy(KTs[e + 1][0:QROW, :], S[1][QROW:2 * QROW, :]).then_inc(s("stacks_second"), 1)

            def maxima(h, k0, k1):
                for k in range(k0, k1):
                    t, c, n = PIECES[k]
                    dve.wait_ge(s("piece_done"), NP * h + k + 1)
                    nc.vector.tensor_reduce(mx2[:, t, c:c + 1], mbank(k)[:, 0:n], AX.X, ALU.max, negate=True
                                            ).then_inc(s("reduced"), 1)

            def maximum(h, e):
                dve.wait_ge(s("reduced"), NP * h + NP)
                nc.vector.tensor_tensor(mx[:, e % 2, :], mx2[:, :, 0], mx2[:, :, 1], ALU.min
                                        ).then_inc(s("max_ready"), 1)

            def sum_rows(i, half):
                dve.wait_ge(s("rows_done"), 2 * i - 1 + half)
                if half == 0 and not (isinstance(i, int) and i < 2):
                    dve.wait_ge(s("rows_scaled"), i - 1)
                nc.vector.tensor_reduce(orow[:, 4 * half:4 * half + 4, :],
                                        R[half].rearrange("p (t c d) -> p t d c", t=4, c=4)[:, :, 0:V1, :],
                                        AX.X, ALU.add).then_inc(s("rows_summed"), 1)

            def scale_rows(i):
                dve.wait_ge(s("rows_summed"), 2 * i)
                nc.vector.reciprocal(rsum[:, :, :], orow[:, :, DH1:V1]).then_inc(s("rsum_ready"), 1)
                dve.wait_ge(s("rsum_ready"), i)
                cols = slice((i - 1) * DH1, i * DH1) if isinstance(i, int) else bass.ds((i - 1) * DH1, DH1)
                nc.vector.tensor_tensor(attn[:, :, cols], orow[:, :, 0:DH1], rsum[:, :, :].to_broadcast([P, NT, DH1]),
                                        ALU.mult).then_inc(s("rows_scaled"), 1)

            def step(i, e, pair=None, first=False, ahead=2, g=None):
                if pair is not None:
                    stacks(pair, (e + 2) % 4)
                if ahead >= 1:
                    take_max_row(i + 1, e + 1, g)
                if ahead == 2:
                    maxima(i + 2, 0, 10)
                if not first:
                    sum_rows(i, 0)
                if ahead == 2:
                    maxima(i + 2, 10, 11)
                if not first:
                    sum_rows(i, 1)
                if ahead == 2:
                    maxima(i + 2, 11, NP)
                    maximum(i + 2, e)
                if not first:
                    scale_rows(i)

            def take_max_row(i, e1, g):
                dve.wait_ge(s("max_turned"), i + 1)
                if g is not None:
                    dve.wait_ge(s(f"max_in{e1 % 2}"), 32 * g + 16 * (e1 // 2))
                elif i >= 2:
                    dve.wait_ge(s(f"max_in{i % 2}"), 16 * (i // 2))
                nc.vector.tensor_copy(crow[:, e1 % 2, :], M[0][0:NT, 0:P]).then_inc(s("crow_ready"), 1)

            stacks(0, 0)
            maxima(0, 0, NP)
            maximum(0, 0)
            take_max_row(0, 0, None)
            maxima(1, 0, NP)
            maximum(1, 1)
            for e in range(4):
                step(e, e, 1 + e // 2 if e % 2 == 0 else None, e == 0)
            with dve.Fori(1, GROUPS - 1) as g:
                for e in range(4):
                    step(4 * g + e, e, 2 * g + 1 + e // 2 if e % 2 == 0 else None, g=g)
            for e in range(4):
                step(H1 - 4 + e, e, H1 // 2 - 1 if e == 0 else None, ahead=min(2, 3 - e))
            for half in range(2):
                sum_rows(H1, half)
            scale_rows(H1)
            dve.wait_ge(s("rows_scaled"), H1)

        @block.tensor
        def _(pe):
            pe.wait_ge(s("o_clear"), 1)
            pe.wait_ge(s("act_const"), 3)

            def turn(p, i):
                pe.wait_ge(s("gathered"), 4 * p + 4)
                for src, out, exps in ((qs, S[0], -1), (ks, S[1], 0)):
                    if i is not None:
                        pe.wait_ge(s("exp_done"), 8 * i + exps)
                    for t in range(NT):
                        last = nc.tensor.transpose(out[:, t * P:(t + 1) * P],
                                                   src[:, t, :, :, :].rearrange("p a b d -> p (a b d)"), ident[:, :])
                    last.then_inc(s("turned"), 1)

            def piece(h, e, k):
                t, c, n = PIECES[k]
                out = mbank(k)
                if k == 1:
                    pe.wait_ge(s("crow_ready"), h)
                elif k >= 2:
                    pe.wait_ge(s("reduced"), NP * h + k - 1)
                diagonal = t // 4 == c
                n = max(n, 2 * P)
                last = nc.tensor.matmul(out[:, 0:n], QT[e][:, t * P:(t + 1) * P],
                                        KTs[e][:, c * BANK:c * BANK + n], start=True, stop=not diagonal)
                if diagonal:
                    d = t * P - c * BANK
                    last = nc.tensor.matmul(out[:, d:d + P], identb[:, :], mask[:, 0, :], start=False, stop=True)
                last.then_inc(s("piece_done"), 1)

            def stacks_ready(pair):
                pe.wait_ge(s("stacks_first"), 2 * pair + 2)
                pe.wait_ge(s("stacks_second"), 2 * pair + 2)

            def aug_ready(h):
                pe.wait_ge(s("qaug"), h + 1)
                if isinstance(h, int) and 1 <= h < 4:
                    pe.wait_ge(s("act_const"), min(h + 3, 6))

            def turn_max(h, e):
                pe.wait_ge(s("max_ready"), h + 1)
                nc.tensor.transpose(M[0][0:NT, 0:P], mx[:, e % 2, :], ident[:, :]).then_inc(s("max_turned"), 1)

            def score(i, e, kt, drained):
                for count in drained:
                    pe.wait_ge(*count)
                if kt >= 2:
                    pe.wait_ge(s("exp_done"), 8 * i + kt - 1)
                out = S[kt % 2]
                spans = [(kt * P, BANK), (BANK, T)] if kt < 4 else [(kt * P, T)]
                for n, (q0, q1) in enumerate(spans):
                    w0 = min(q0, q1 - 2 * P)
                    last = nc.tensor.matmul(out[:, w0:q1], KTs[e][:, kt * P:(kt + 1) * P], QT[e][:, w0:q1],
                                            start=True, stop=n == 1)
                    if n == 0:
                        last = nc.tensor.matmul(out[:, q0:q0 + P], identb[:, :], mask[:, 1, :], start=False, stop=True)
                last.then_inc(s("scored"), 1)

            def values(i, e, g, part):
                b, vb = (e - 1) % 2, (e - 1) % 4
                if part == 0:
                    pe.wait_ge(s("exp_done"), 8 * i)
                    pe.wait_ge(s("v_gathered"), 2 * g + (e + 1) // 2)
                    if not (isinstance(i, int) and i < 2):
                        pe.wait_ge(s("o_taken"), i - 1)
                c = min(part, 1)
                for kt in range(4, NT) if part == 2 else range(4):
                    cls = slice(32 * (kt % 4), 32 * (kt % 4) + V1)
                    q0, q1 = max(c * BANK, kt * P), (c + 1) * BANK
                    last = nc.tensor.matmul(O[cls, q0:q1], vs[:, vb // 2, kt, (vb % 2) * V1:(vb % 2 + 1) * V1],
                                            pr[b][kt][:, q0 - kt * P:q1 - kt * P], start=kt < 4,
                                            stop=part == 0 or part == 2, tile_position=(0, 32 * (kt % 4)))
                if part == 2:
                    last.then_inc(s("values_done"), 1)

            def output_rows(i, half):
                if half == 0:
                    pe.wait_ge(s("o_taken"), i)
                for t in range(4):
                    q = (4 * half + t) * P
                    last = nc.tensor.transpose(R[half][:, t * P:(t + 1) * P], osb[:, q:q + P], ident[:, :])
                last.then_inc(s("rows_done"), 1)

            def step(i, e, g, first=False, ahead=2, turning=True):
                e2, pair = (e + 2) % 4, 2 * g + e // 2
                if not (isinstance(i, int) and i < 2):
                    pe.wait_ge(s("rows_summed"), 2 * i - 2)
                if e % 2 == 0 and turning:
                    turn(pair + 1, None if first else i)
                    if not first:
                        values(i, e, g, 0)
                    drained = [[(s(f"stacks_{n}"), 2 * pair + 3 + kt) for n in ("first", "second")] for kt in range(2)]
                else:
                    drained = [[(s("exp_done"), 8 * i - 1 + kt)] for kt in range(2)]
                pe.wait_ge(s(f"max_in{e % 2}"), 32 * g + 16 * (e // 2 + 1))
                order = [(), (0, 1), (2, 3), (4, 5), (6, 7), (8, 9), (10,), (11,)]
                for kt in range(NT):
                    score(i, e, kt, drained[kt] if kt < 2 else ())
                    if (1 if e % 2 == 0 and turning else 0) <= kt < 3 and not first:
                        values(i, e, g, kt)
                    if kt == 0 and ahead >= 1:
                        turn_max(i + 1, (e + 1) % 4)
                    if kt == 1 and ahead == 2:
                        aug_ready(i + 2)
                    if kt in (5, 6) and not first:
                        output_rows(i, kt - 5)
                    if ahead == 2:
                        for k in order[kt]:
                            piece(i + 2, e2, k)

            turn(0, None)
            stacks_ready(0)
            aug_ready(0)
            for k in range(NP):
                piece(0, 0, k)
            turn_max(0, 0)
            aug_ready(1)
            for k in range(NP):
                piece(1, 1, k)
            for e in range(4):
                step(e, e, 0, first=e == 0)
            with pe.Fori(1, GROUPS - 1) as g:
                for e in range(4):
                    step(4 * g + e, e, g)
            for e in range(4):
                i = H1 - 4 + e
                step(i, e, GROUPS - 1, ahead=min(2, 3 - e), turning=e == 0)
            for part in range(3):
                values(H1, 0, GROUPS, part)
            pe.wait_ge(s("rows_summed"), 2 * H1 - 2)
            output_rows(H1, 0)
            output_rows(H1, 1)


def attention1_out(nc, top, attn, w_dram):
    ctx = ExitStack()
    with ctx:
        def sb(name, shape, dt=F32):
            return ctx.enter_context(nc.sbuf_tensor(f"a1o_{name}", shape, dt))
        s = Sems(nc, ctx, "a1o")
        ps = ctx.enter_context(nc.psum_tensor("a1o_ps", [P, 8, BANK], F32))
        t_h, t_l = sb("t_h", [P, KT, T], F32R), sb("t_l", [P, KT, T], F32R)
        raw = sb("raw", [P, KT * D])
        w_h, w_l = sb("w_h", [P, KT * D], F32R), sb("w_l", [P, KT * D], F32R)
        x = top["x"]
        block = ctx.enter_context(nc.Block())
        bank = lambda t: ps[:, t, :].rearrange("p (k q) -> p k q", k=KT)

        @block.sync
        def _(sp):
            sp.dma_start(raw[:, :], w_dram).then_inc(s("raw_in"), 16)

        @block.gpsimd
        def _(pool):
            pool.wait_ge(s("raw_in"), 16)
            split_hi(nc.gpsimd, w_h[:, :], raw[:, :]).then_inc(s("w_hi"), 1)
            pool.wait_ge(s("w_hi"), 1)
            nc.gpsimd.tensor_tensor(w_l[:, :], raw[:, :], w_h[:, :], ALU.subtract).then_inc(s("w_split"), 1)

        @block.scalar
        def _(act):
            for t in range(NT):
                act.wait_ge(s("turned"), t + 1)
                nc.scalar.copy(t_h[:, :, t * P:(t + 1) * P], bank(t)).then_inc(s("hi"), 1)

        @block.vector
        def _(dve):
            for t in range(NT):
                dve.wait_ge(s("hi"), t + 1)
                nc.vector.tensor_tensor(t_l[:, :, t * P:(t + 1) * P], bank(t), t_h[:, :, t * P:(t + 1) * P],
                                        ALU.subtract).then_inc(s("lo"), 1)
            for t in range(NT):
                dve.wait_ge(s("out_done"), t + 1)
                nc.vector.tensor_tensor(x[:, t, :], x[:, t, :], ps[:, t, :], ALU.add).then_inc(s("added"), 1)
            dve.wait_ge(s("added"), NT)

        @block.tensor
        def _(pe):
            for t in range(NT):
                for k in range(KT):
                    last = nc.tensor.transpose(ps[:, t, k * P:(k + 1) * P], attn[:, t, k * P:(k + 1) * P],
                                               top["ident"][:, :])
                last.then_inc(s("turned"), 1)
            pe.wait_ge(s("w_split"), 1)
            for t in range(NT):
                pe.wait_ge(s("lo"), t + 1)
                q = slice(t * P, (t + 1) * P)
                for k in range(KT):
                    w = slice(k * D, (k + 1) * D)
                    last = mm3(nc, ps[:, t, :], t_h[:, k, q], t_l[:, k, q], w_h[:, w], w_l[:, w],
                               k == 0, k == KT - 1)
                last.then_inc(s("out_done"), 1)


def stage_ffn1(nc, top, w1_dram, w2_dram, b1_dram, b2_dram, out_dram):
    ctx = ExitStack()
    with ctx:
        def sb(name, shape, dt=F32):
            return ctx.enter_context(nc.sbuf_tensor(f"f1_{name}", shape, dt))
        s = Sems(nc, ctx, "f1")
        ps = ctx.enter_context(nc.psum_tensor("f1_ps", [P, 8, BANK], F32))
        OUT = 4
        xh_h, xh_l = sb("xh_h", [P, KT, T], F32R), sb("xh_l", [P, KT, T], F32R)
        raw = {w: sb(f"raw{w}", [P, 2, 512]) for w in (1, 2)}
        w_h = {w: sb(f"w{w}_h", [P, 2, 512], F32R) for w in (1, 2)}
        w_l = {w: sb(f"w{w}_l", [P, 2, 512], F32R) for w in (1, 2)}
        b1 = sb("b1", [P, NF1])
        b2 = sb("b2", [P, D])
        h = sb("h", [P, 2, BANK])
        h_h, h_l = sb("h_h", [P, 2, BANK], F32R), sb("h_l", [P, 2, BANK], F32R)
        x = top["x"]
        b = dict(top, ps=ps, xh_h=xh_h, xh_l=xh_l, xn=sb("xn", [P, 2, D]))
        block = ctx.enter_context(nc.Block())
        w_dram = {1: w1_dram, 2: w2_dram}
        PAIRS = NF1 // 2

        @block.sync
        def _(sp):
            sp.dma_start(b1[:, :], b1_dram).then_inc(s("b_in"), 16)
            sp.dma_start(b2[:, :], b2_dram.to_broadcast([P, D])).then_inc(s("b_in"), 16)
            for half in range(2):
                for w in (1, 2):
                    for i in range(2):
                        if half:
                            sp.wait_ge(s(f"w{w}_split"), NF1 - 1 + i)
                        sp.dma_start(raw[w][:, i, :], w_dram[w][i]).then_inc(s(f"raw{w}_in{i}"), 16)
                with sp.Fori(1, PAIRS) as f2:
                    for i in range(2):
                        for w in (1, 2):
                            sp.wait_ge(s(f"w{w}_split"), 2 * f2 + i - 1 + half * NF1)
                            sp.dma_start(raw[w][:, i, :], w_dram[w][2 * f2 + i]).then_inc(s(f"raw{w}_in{i}"), 16)
            for t in range(NT):
                sp.wait_ge(s("out_added"), t + 1)
                sp.dma_start(out_dram[t * P:(t + 1) * P, :], x[:, t, :]).then_inc(s("stored"), 16)
            sp.wait_ge(s("stored"), 16 * NT)

        @block.gpsimd
        def _(pool):
            def split(w, turn, i, used=None):
                pool.wait_ge(s(f"raw{w}_in{i}"), 16 * turn + 16)
                if used is not None:
                    pool.wait_ge(s(used), 2 * turn + i - 1)
                take_wait(nc, top, turn)
                split_hi(nc.gpsimd, w_h[w][:, i, :], raw[w][:, i, :]).then_inc(s(f"w{w}_hi"), 1)
                pool.wait_ge(s(f"w{w}_hi"), 2 * turn + i + 1)
                nc.gpsimd.tensor_tensor(w_l[w][:, i, :], raw[w][:, i, :], w_h[w][:, i, :], ALU.subtract
                                        ).then_inc(s(f"w{w}_split"), 1)

            for t in range(4):
                ln_gpsimd(nc, pool, s, b, t)
            split(1, 0, 0)
            for t in range(4, NT):
                ln_gpsimd(nc, pool, s, b, t)
            split(1, 0, 1)
            split(2, 0, 0)
            split(2, 0, 1)
            pool.wait_ge(s("b_in"), 32)
            pool.wait_ge(s("ln_normed"), NT)
            for t in range(NT):
                nc.gpsimd.tensor_tensor(x[:, t, :], x[:, t, :], b2[:, :], ALU.add).then_inc(s("b2_added"), 1)
            with pool.Fori(1, NF1) as turn:
                for i in range(2):
                    split(1, turn, i, "h_done")
                    split(2, turn, i, "out_step")

        @block.scalar
        def _(act):
            ln_scalar(nc, act, s, b)
            act.wait_ge(s("b_in"), 32)

            def gelu(n, i, bias):
                act.wait_ge(s("h_done"), n + 1)
                if not (isinstance(n, int) and n < 2):
                    act.wait_ge(s("h_split"), n - 1)
                nc.scalar.activation(h[:, i, :], ps[:, i, :], ACT.Gelu_apprx_tanh, bias=bias
                                     ).then_inc(s("h_ready"), 1)

            for half in range(2):
                for i in range(2):
                    gelu(i + half * NF1, i, b1[:, i:i + 1])
                with act.Fori(1, PAIRS) as f2:
                    for i in range(2):
                        gelu(2 * f2 + i + half * NF1, i, b1[:, bass.ds(2 * f2 + i, 1)])

        @block.vector
        def _(dve):
            ln_vector(nc, dve, s, b)

            def split(n, i):
                dve.wait_ge(s("h_ready"), n + 1)
                if not (isinstance(n, int) and n < 2):
                    dve.wait_ge(s("out_step"), n - 1)
                nc.vector.tensor_copy(h_h[:, i, :], h[:, i, :]).then_inc(s("h_hi"), 1)
                dve.wait_ge(s("h_hi"), n + 1)
                nc.vector.tensor_tensor(h_l[:, i, :], h[:, i, :], h_h[:, i, :], ALU.subtract).then_inc(s("h_split"), 1)

            for half in range(2):
                for i in range(2):
                    split(i + half * NF1, i)
                with dve.Fori(1, PAIRS) as f2:
                    for i in range(2):
                        split(2 * f2 + i + half * NF1, i)
                dve.wait_ge(s("out_step"), (half + 1) * NF1)
                dve.wait_ge(s("b2_added"), NT)
                for i in range(4):
                    t = 4 * half + i
                    nc.vector.tensor_tensor(x[:, t, :], x[:, t, :], ps[:, OUT + i, :], ALU.add
                                            ).then_inc(s("out_added"), 1)

        @block.tensor
        def _(pe):
            ln_tensor(nc, pe, s, b, range(4))
            pe.wait_ge(s("ln_lo"), 4)

            def hidden(n, half, i):
                pe.wait_ge(s("w1_split"), n + 1)
                if not (isinstance(n, int) and n < 2):
                    pe.wait_ge(s("h_ready"), n - 1)
                q = slice(half * BANK, (half + 1) * BANK)
                for k in range(KT):
                    c = slice(k * P, (k + 1) * P)
                    last = mm3(nc, ps[:, i, :], w_h[1][:, i, c], w_l[1][:, i, c], xh_h[:, k, q], xh_l[:, k, q],
                               k == 0, k == KT - 1)
                last.then_inc(s("h_done"), 1)

            def out(n, i, start, stop):
                pe.wait_ge(s("h_split"), n)
                pe.wait_ge(s("w2_split"), n)
                for j in range(4):
                    t = slice(j * P, (j + 1) * P)
                    last = mm3(nc, ps[:, OUT + j, :], h_h[:, i, t], h_l[:, i, t], w_h[2][:, i, :], w_l[2][:, i, :],
                               start, stop)
                last.then_inc(s("out_step"), 1)

            for half in range(2):
                n0 = half * NF1
                hidden(n0, half, 0)
                if half:
                    out(n0, 1, False, True)
                hidden(n0 + 1, half, 1)
                if half:
                    pe.wait_ge(s("out_added"), 4)
                else:
                    ln_tensor(nc, pe, s, b, range(4, NT))
                    pe.wait_ge(s("ln_lo"), NT)
                out(n0 + 1, 0, True, False)
                with pe.Fori(1, PAIRS) as f2:
                    for i in range(2):
                        hidden(2 * f2 + i + n0, half, i)
                        out(2 * f2 + i + n0, 1 - i, False, False)
            out(2 * NF1, 1, False, True)


def program(nc, a, out):
    ctx = ExitStack()
    with ctx:
        def sb(name, shape, dt=F32):
            return ctx.enter_context(nc.sbuf_tensor(name, shape, dt))
        top = {
            "x": sb("x", [P, NT, D]), "ident": sb("ident", [P, P]),
            "ident_dram": a["ident_in"], "neg_half": sb("neg_half", [P, 32]), "tick": sb("tick", [P, 1]),
            "stats": sb("stats", [P, NT, 6]), "meanvar": sb("meanvar", [P, NT, 2]),
            "var_eps": sb("var_eps", [P, NT]), "rstd": sb("rstd", [P, NT]), "shift": sb("shift", [P, NT]),
        }
        stage_attention0(nc, top, a["x_in"], a["a0_wqkgv"], a["a0_wout"], a["a0_cst"], a["a0_normw"])
        stage_ffn0(nc, top, a["f0_w1"], a["f0_w3"], a["f0_w2"], a["f0_lora_a"], a["f0_lora_b2"])
        stage_attention1(nc, top, a)
        stage_ffn1(nc, top, a["f1_w1"], a["f1_w2"], a["f1_b1"], a["f1_b2"], out)


def decays():
    import numpy as np
    base = 1.0 / 2.0 ** (8.0 / H0)
    slope = base ** (np.arange(H0) + 1.0) * (1.0 - 1 / (31 + 1e-05) + 1e-05)
    n = np.arange(P)
    c = np.zeros((H0, P, CST))
    for h in range(H0):
        gap = n[None, :] - n[:, None]
        c[h, :, 0:P] = np.where(gap >= 0, np.exp(-slope[h] * np.maximum(gap, 0)), 0.0)
        c[h, :, P:2 * P] = np.exp(-slope[h] * (n + 1.0))[None, :]
        c[h, :, 2 * P] = np.exp(-slope[h] * (P - 1.0 - n))
        c[h, :, 2 * P + 1] = np.exp(-slope[h] * P)
    return c.astype(np.float32).reshape(NG, G4, P, CST)


def alibi():
    import numpy as np
    pos = np.arange(T)
    rows = ROWS - QROW
    aug = np.zeros((rows, 2, T), np.float32)
    for r in range(2 * NT):
        aug[r, 0] = 4.0 * (pos - P * (r % NT))
        aug[r, 1] = pos // P == r % NT
    aug[MAXROW - QROW, 0] = 1.0
    slopes = (1.0 / 2.0 ** (np.arange(1, H1 + 1) * (8.0 / H1))).astype(np.float32)
    hi = (slopes.view(np.uint32) & np.uint32(0xFFFFF000)).view(np.float32)
    slope = np.zeros((rows, H1), np.float32)
    slope[0:NT], slope[NT:2 * NT] = hi, slopes - hi
    n = np.arange(P)
    later = np.where(n[None, :] > n[:, None], -BIG, 0.0).astype(np.float32)
    return {"a1_aug": aug, "a1_slope": slope, "a1_mask": np.stack([later, later.T], axis=1)}


def arrange(inputs):
    import numpy as np
    f = {k: np.asarray(v) for k, v in inputs.items()}
    qkv = f["L0_attn_qkv_w"].reshape(NG, G4, 3, DH0, KT, P)
    gate = f["L0_attn_gate_w"].reshape(NG, G4, DH0, KT, P)
    across = lambda w: w.transpose(0, 1, 4, 3, 2).reshape(NG, G4, P, 512)
    v = qkv[:, :, 2].transpose(0, 3, 4, 1, 2).reshape(NG, KT, P, 512)
    pad = lambda w: np.pad(w, ((0, NF0 * P - F0), (0, 0)))

    def stacked(w, rows):
        out = np.zeros((rows, w.shape[1]), np.float32)
        for at in (0, 32, 64):
            out[at:at + w.shape[0]] = w
        return out

    def hidden_tiles(w, lora_b):
        t = pad(w).reshape(NF0, P, KT, P).transpose(0, 3, 2, 1).reshape(NF0, P, 512)
        lb = stacked(pad(lora_b).T, P).reshape(P, NF0, P).transpose(1, 0, 2)
        return np.concatenate([t, lb], axis=-1)

    w2 = pad(f["L0_ffn_w2"].T).reshape(NF0, P, D)
    a2 = stacked(pad(f["L0_ffn_lora_A2"].T).T, P).reshape(P, NF0, P).transpose(1, 0, 2)
    lora_a = [stacked(f[n], LR).reshape(LR, KT, P).transpose(2, 1, 0) for n in ("L0_ffn_lora_A1", "L0_ffn_lora_A3")]
    return {
        "f0_w1": hidden_tiles(f["L0_ffn_w1"], f["L0_ffn_lora_B1"]),
        "f0_w3": hidden_tiles(f["L0_ffn_w3"], f["L0_ffn_lora_B3"]),
        "f0_w2": np.concatenate([w2, a2], axis=-1),
        "f0_lora_a": np.stack(lora_a, axis=1),
        "f0_lora_b2": stacked(f["L0_ffn_lora_B2"].T, LR),
        "a1_wqkv": f["L1_attn_w_qkv"].T.reshape(KT, P, 3, D).transpose(2, 1, 0, 3).reshape(3, P, KT * D),
        "a1_ln": np.stack([f[f"L1_attn_{n}"] for n in ("q_ln_w", "q_ln_b", "k_ln_w", "k_ln_b")]),
        "a1_wout": f["L1_attn_w_out"].T.reshape(KT, P, D).transpose(1, 0, 2).reshape(P, KT * D),
        **alibi(),
        "f1_w1": f["L1_ffn_inter_w"].reshape(KT, P, NF1, P).transpose(2, 1, 0, 3).reshape(NF1, P, 512),
        "f1_w2": f["L1_ffn_output_w"].reshape(NF1, P, D),
        "f1_b1": f["L1_ffn_inter_b"].reshape(NF1, P).T,
        "f1_b2": f["L1_ffn_output_b"].reshape(1, D),
        "x_in": f["L0_attn_hidden_states"].reshape(T, D),
        "ident_in": np.eye(P, dtype=np.float32),
        "a0_wqkgv": np.concatenate([across(qkv[:, :, 0]), across(qkv[:, :, 1]), across(gate), v], axis=-1),
        "a0_wout": f["L0_attn_out_w"].T.reshape(NG, G4, DH0, D),
        "a0_cst": decays(),
        "a0_normw": f["L0_attn_norm_w"].reshape(H0, DH0).T,
    }


def kernel(**inputs):
    import numpy as np
    import concourse.bacc as bacc
    from concourse.bass_utils import run_bass_kernel_spmd
    nc = bacc.Bacc("TRN2", target_bir_lowering=False, num_devices=1)
    arrays, args = {}, {}
    for name, value in arrange(inputs).items():
        arrays["in_" + name] = np.ascontiguousarray(value)
        args[name] = nc.dram_tensor("in_" + name, value.shape, F32, kind="ExternalInput").ap()
    out = nc.dram_tensor("out_0", (T, D), F32, kind="ExternalOutput").ap()
    program(nc, args, out)
    result = run_bass_kernel_spmd(nc, [arrays], core_ids=[0])
    return result.results[0]["out_0"].reshape(1, T, D)
```
